# Optimizing a Trainium2 kernel written in Bass

```python
import numpy as np
import jax
import jax.numpy as jnp

def _softmax(x, axis=-1):
    return jax.nn.softmax(x, axis=axis)

def _gelu(x):
    return jax.nn.gelu(x, approximate=True)

def _silu(x):
    return jax.nn.silu(x)

def _sigmoid(x):
    return jax.nn.sigmoid(x)

def _layernorm(x, axis=-1, eps=1e-05):
    m = jnp.mean(x, axis=axis, keepdims=True)
    v = jnp.var(x, axis=axis, keepdims=True)
    return (x - m) / jnp.sqrt(v + eps)

def _scatter_add(tgt, idx, src, axis=0):
    return tgt.at[idx].add(src)

def _segment_sum(src, seg, n):
    return jax.ops.segment_sum(src, seg, n)
kernel_name = 'mk_adj_preln_d2_adj_r2_659172'

def setup_inputs(seed: int=0):
    np.random.seed(seed)
    _w = jnp.asarray

    def _rec_inputs():
        import jax
        import jax.numpy as jnp
        _gk = jax.random.key(seed)
        x = -0.0005207 + 1.001 * jax.random.normal(jax.random.fold_in(_gk, 1), (8192, 128), jnp.float32)
        _a = jax.random.bernoulli(jax.random.fold_in(_gk, 2), 0.00195312, (8192, 8192))
        _a = jnp.logical_or(_a, jnp.swapaxes(_a, -1, -2))
        _a = jnp.logical_or(_a, jnp.eye(8192, dtype=bool))
        _af = _a.astype(jnp.float32)
        adj = _af
        return (x, adj)
    x, adj = _rec_inputs()

    def _L0_gnn_setup():
        import jax, jax.numpy as jnp
        import numpy as np
        N = 4096
        D = 128
        ALPHA = 0.2
        NEG_INF = -9000000000000000.0
        key = jax.random.key(seed)
        k1, k2, k3, k4, k5, k6 = jax.random.split(key, 6)
        inputs = jax.random.normal(k1, (N, D), dtype=jnp.float32)
        adj = (jax.random.uniform(k2, (N, N)) < 32.0 / N).astype(jnp.float32)
        adj = jnp.maximum(adj, jnp.eye(N, dtype=jnp.float32))
        cmt_weight = jax.random.uniform(k3, (N, 1), dtype=jnp.float32)
        W = jax.random.normal(k4, (D, D), dtype=jnp.float32) * (1.0 / np.sqrt(D))
        a1 = jax.random.normal(k5, (D, 1), dtype=jnp.float32) * 0.1
        a2 = jax.random.normal(k6, (D, 1), dtype=jnp.float32) * 0.1
        return {'inputs': inputs, 'adj': adj, 'cmt_weight': cmt_weight, 'W': W, 'a1': a1, 'a2': a2}
    _L0_gnn_all = _L0_gnn_setup()
    _L0_gnn_in = {k: v for k, v in _L0_gnn_all.items() if k in ('cmt_weight', 'W', 'a1', 'a2')}
    del _L0_gnn_all

    def _L1_gnn_setup():
        import jax, jax.numpy as jnp
        import numpy as np
        N = 10000
        D = 128
        F = 128
        K = F // 8
        key = jax.random.key(seed)
        k1, k2, k3, k4, k5 = jax.random.split(key, 5)
        h = jax.random.normal(k1, (N, D), dtype=jnp.float32)
        adj = jax.random.uniform(k2, (N, N), dtype=jnp.float32)
        W1 = jax.random.normal(k3, (D, K), dtype=jnp.float32) * 0.05
        W2 = jax.random.normal(k4, (K, D, F), dtype=jnp.float32) * 0.05
        b = jax.random.normal(k5, (K, F), dtype=jnp.float32) * 0.05
        return {'h': h, 'adj': adj, 'W1': W1, 'W2': W2, 'b': b}
    _L1_gnn_all = _L1_gnn_setup()
    _L1_gnn_in = {k: v for k, v in _L1_gnn_all.items() if k in ('W1', 'W2', 'b')}
    del _L1_gnn_all
    return {'x': x, 'adj': adj, 'L0_gnn_cmt_weight': _L0_gnn_in['cmt_weight'], 'L0_gnn_W': _L0_gnn_in['W'], 'L0_gnn_a1': _L0_gnn_in['a1'], 'L0_gnn_a2': _L0_gnn_in['a2'], 'L1_gnn_W1': _L1_gnn_in['W1'], 'L1_gnn_W2': _L1_gnn_in['W2'], 'L1_gnn_b': _L1_gnn_in['b']}

def reference(x, adj, L0_gnn_cmt_weight, L0_gnn_W, L0_gnn_a1, L0_gnn_a2, L1_gnn_W1, L1_gnn_W2, L1_gnn_b):
    import jax
    import jax.numpy as jnp

    def _L0_gnn_ref(inputs, adj, cmt_weight, W, a1, a2):
        import jax, jax.numpy as jnp
        import numpy as np
        N = 4096
        D = 128
        ALPHA = 0.2
        NEG_INF = -9000000000000000.0
        Wh = inputs @ W
        f1 = Wh @ a1
        f2 = Wh @ a2
        e = jax.nn.leaky_relu(f1 + f2.T, negative_slope=ALPHA)
        scores = jnp.where(adj > 0, e, NEG_INF)
        att = jax.nn.softmax(scores, axis=-1)
        node_out = jax.nn.relu(att @ Wh)
        return node_out

    def _L1_gnn_ref(h, adj, W1, W2, b):
        import jax, jax.numpy as jnp
        import numpy as np
        N = 10000
        D = 128
        F = 128
        K = F // 8
        node = h @ W1
        hw = jnp.einsum('nc,kcf->nkf', h, W2)
        x = jnp.einsum('nk,nkf->nf', node, hw)
        x = adj @ x
        x = x + node @ b
        return jax.nn.relu(x)
    h = jnp.maximum(_layernorm(x, axis=-1), 0.0)
    x = x + _L0_gnn_ref(h, adj, L0_gnn_cmt_weight, L0_gnn_W, L0_gnn_a1, L0_gnn_a2)
    h = jnp.maximum(_layernorm(x, axis=-1), 0.0)
    x = x + _L1_gnn_ref(h, adj, L1_gnn_W1, L1_gnn_W2, L1_gnn_b)
    return x

_drawn_inputs = setup_inputs


def setup_inputs(seed=0):
    import zlib

    import numpy as np

    out = dict(_drawn_inputs(seed))
    spreads = {}
    factors = {'L0_gnn_a1': 6.427, 'L1_gnn_b': 6.357}
    for name, (base, spread) in spreads.items():
        noise = np.random.default_rng([zlib.crc32(name.encode()), seed]).standard_normal(out[name].shape)
        drawn = base * np.exp(spread * noise) if base else spread * noise
        out[name] = jnp.asarray(drawn.astype(out[name].dtype))
    for name, factor in factors.items():
        out[name] = (out[name] * factor).astype(out[name].dtype)
    return out
```

```python
from contextlib import ExitStack

import concourse.bass as bass
from concourse import mybir

FP32 = mybir.dt.float32
BF16 = mybir.dt.bfloat16
FP8 = mybir.dt.float8e4
U8 = mybir.dt.uint8
U16 = mybir.dt.uint16
ALU = mybir.AluOpType
ACT = mybir.ActivationFunctionType
AX = mybir.AxisListType

EPS = 1e-5
SLOPE = 0.2
EDGE = 64.0
EDGE_FP8 = 2.0


def build(nc, x, adj, W, a1, a2, W1, W2, b, out):
    N, D = x.shape
    K = W1.shape[1]
    P = 128
    T = 8
    BLK = P * T
    NB = N // BLK
    NT = NB * T
    C = T // 2
    HB = 512
    IT = NB // 2
    HT = T // 2
    assert NB == T and BLK == 2 * HB and D == P

    adj_v = adj.rearrange("(i p t) n -> i p t n", p=P, t=T)
    x_v = x.rearrange("(i p t) f -> i p t f", p=P, t=T)
    out_v = out.rearrange("(i p t) f -> i p t f", p=P, t=T)

    zrow_d = nc.dram_tensor("zrow_d", [NT, P], FP32).ap()
    maskT_d = nc.dram_tensor("maskT_d", [NB, NB, P, C * BLK], U16).ap()
    msg_d = nc.dram_tensor("msg_d", [P, NT, 3 * D], BF16).ap()
    keep_d = nc.dram_tensor("keep_d", [P, NT, 2 * D], FP32).ap()

    ctx = ExitStack()
    with ctx:
        def sb(name, shape, dt=FP32):
            return ctx.enter_context(nc.sbuf_tensor(name, shape, dt))

        def bank(name):
            return ctx.enter_context(nc.psum_tensor(name, [P, HB], FP32))

        def sem(name):
            return ctx.enter_context(nc.semaphore(name))

        adj_sb = sb("adj_sb", [P, 4, HT * BLK])
        wh_mask = sb("wh_mask", [P, NT * D + BLK * T // 2])
        p_sb = sb("p_sb", [P, 4, BLK])
        prod = sb("prod", [P, K, D])
        zb = sb("zb", [P, 2, BLK])
        mt = sb("mt", [P, 2, C, BLK], U16)
        whs = sb("whs", [P, 2, T, D])
        acc = sb("acc", [P, 2, BLK])
        ut = sb("ut", [P, BLK])
        wcat = sb("wcat", [P, K * D + K + D])
        w_sb = sb("w_sb", [P, D])
        wa = sb("wa", [P, 2])
        a12 = sb("a12", [P, 2])
        b_sb = sb("b_sb", [K, D])
        tr_sb = sb("tr_sb", [P, D])
        ident = sb("ident", [P, P])
        ident16 = sb("ident16", [P, P], BF16)
        zeros16 = sb("zeros16", [P, HB], BF16)
        ones = sb("ones", [P, P])
        eps = sb("eps", [P, 1])
        xt = sb("xt", [P, T, D])
        ustat = sb("ustat", [P, P])
        keep = sb("keep", [P, 2, 2 * D])
        msg = sb("msg", [P, 2, 3 * D], BF16)
        msg32 = sb("msg32", [P, 2, D])
        xn = sb("xn", [P, D])
        hT = sb("hT", [P, D])
        node = sb("node", [P, K])
        att = sb("att", [P, D])
        stat = sb("stat", [P, 6])
        mv = sb("mv", [P, 2])
        std = sb("std", [P, 1])
        rstd = sb("rstd", [P, 1])
        fcol = sb("fcol", [P, NT, 2])
        bcol = sb("bcol", [P, NT])
        qcol = sb("qcol", [P, NT])
        zcol = sb("zcol", [P, NT])
        zT = sb("zT", [NT, P])
        ext = sb("ext", [P, 2])
        extT = sb("extT", [2, P])
        ext2 = sb("ext2", [2, 1])
        extd = sb("extd", [2, 2])
        gmm = sb("gmm", [P, 2])
        shifts = sb("shifts", [P, 3])
        hsum = sb("hsum", [P, 2 * NB])
        hsum1 = sb("hsum1", [P, 1])
        hrep = sb("hrep", [P, P])
        whsum = sb("whsum", [P, D])
        den = sb("den", [P, T])
        empty = sb("empty", [P, T])
        rden = sb("rden", [P, T])

        wh = wh_mask[:, 0:NT * D].rearrange("p (n f) -> p n f", f=D)
        m8 = wh_mask[:, NT * D:].bitcast(U8).rearrange("p (s t n) -> p s t n", s=2, t=T)
        mtb = mt[:, :, :, :].rearrange("p s c n -> p (s c n)").bitcast(U8)\
            .rearrange("p (s c n b) -> p s c n b", s=2, c=C, b=2)
        xn8 = p_sb[:, 0, :].rearrange("p (t f) -> p t f", f=D)
        hT4 = p_sb[:, 2, :].rearrange("p (s n) -> p s n", s=2)
        stat8 = ut[:, 0:T * 6].rearrange("p (t s) -> p t s", t=T)
        mv8 = ut[:, 64:64 + 2 * T].rearrange("p (t s) -> p t s", t=T)
        std8 = ut[:, 96:96 + T]
        rstd8 = ut[:, 112:112 + T]
        msgs = wh_mask[:, :].bitcast(BF16).rearrange("p (n c f) -> p n c f", c=3, f=D)
        masks = adj_sb[:, :, :].rearrange("p s n -> p (s n)").bitcast(FP8)\
            .rearrange("p (s i c n b) -> p s i c n b", s=4, i=2, c=C, b=2)
        masks_w = adj_sb[:, :, :].rearrange("p s n -> p (s n)").bitcast(U16)\
            .rearrange("p (s i w) -> p s i w", s=4, i=2)
        keeps = p_sb[:, :, :].rearrange("p s (n f) -> p (s n) f", f=2 * D)
        yT = prod[:, :, :].rearrange("p k f -> p (k f)")
        outs = zb[:, :, :].rearrange("p s (n f) -> p (s n) f", f=D)

        mt_ps = [bank("mt_ps0"), bank("mt_ps1")]
        ot_ps = [bank("ot_ps0"), bank("ot_ps1")]
        hw_ps = [bank("hw_ps0"), bank("hw_ps1")]
        u_ps = bank("u_ps")
        h_ps = bank("h_ps")
        zbf = zb[:, :, :].rearrange("p s n -> p (s n)")
        acc_ps = [*mt_ps, *ot_ps]
        y_ps = [*hw_ps, u_ps, h_ps]
        DEN = u_ps[:, D:D + T]
        NODE = h_ps[:, D:D + K]
        BIAS = h_ps[:, D + K:D + K + D]

        par_in = sem("par_in")
        w2_in = sem("w2_in")
        x_in = sem("x_in")
        consts = sem("consts")
        setup_pe = sem("setup_pe")
        setup_act = sem("setup_act")
        setup_dve = sem("setup_dve")
        stats8 = sem("stats8")
        mv8_done = sem("mv8_done")
        std8_done = sem("std8_done")
        rstd8_done = sem("rstd8_done")
        xn8_done = sem("xn8_done")
        xnT_done = sem("xnT_done")
        hT_done = sem("hT_done")
        wh_done = sem("wh_done")
        wh_copied = sem("wh_copied")
        wh_scaled = sem("wh_scaled")
        z_stored = sem("z_stored")
        zb_in = sem("zb_in")
        adj_in = [sem(f"adj_in{q}") for q in range(4)]
        adj_cast = [sem(f"adj_cast{q}") for q in range(4)]
        turned = sem("turned")
        evicted = sem("evicted")
        dve_step = [sem("dve_step0"), sem("dve_step1")]
        mt_stored = [sem("mt_stored0"), sem("mt_stored1")]
        p_ready = sem("p_ready")
        p_used = [sem(f"p_used{r}") for r in range(4)]
        whs_ready = [sem("whs_ready0"), sem("whs_ready1")]
        ot_copied = sem("ot_copied")
        acc_clear = sem("acc_clear")
        den_done = sem("den_done")
        den_step = sem("den_step")
        den_read = sem("den_read")
        xt_in = sem("xt_in")
        u_copied = sem("u_copied")
        u_done = sem("u_done")
        u_read = sem("u_read")
        x1_step = sem("x1_step")
        mv_done = sem("mv_done")
        std_done = sem("std_done")
        rstd_done = sem("rstd_done")
        xn_done = sem("xn_done")
        hps_done = sem("hps_done")
        h_done = sem("h_done")
        node_done = sem("node_done")
        node_copied = sem("node_copied")
        hw_done = sem("hw_done")
        hw_scaled = [sem("hw_scaled0"), sem("hw_scaled1")]
        fold_step = sem("fold_step")
        prod_read = sem("prod_read")
        cut_step = sem("cut_step")
        msg_out = [sem("msg_out0"), sem("msg_out1")]
        keep_out = [sem("keep_out0"), sem("keep_out1")]
        msgs_in = [sem(f"msgs_in{s}") for s in range(NB)]
        masks_in = [sem(f"masks_in{q}") for q in range(4)]
        masks_used = [sem(f"masks_used{q}") for q in range(4)]
        keeps_in = sem("keeps_in")
        y_done = sem("y_done")
        y_act = sem("y_act")
        y_dve = sem("y_dve")
        y_turned = sem("y_turned")
        y_step = sem("y_step")
        out_ready = sem("out_ready")
        out_stored = sem("out_stored")

        past_dve = sem("past_dve")
        past_pool = sem("past_pool")
        past_pe = sem("past_pe")

        block = ctx.enter_context(nc.Block())

        def attention_loop(eng, turn, start_block=None, end_block=None):
            def one_block(ib, finish, last):
                if start_block:
                    start_block(ib, last)
                with eng.Fori(0, IT - 1) as jg:
                    turn(ib * IT + jg, ib, jg, finish, False)
                turn(ib * IT + IT - 1, ib, IT - 1, finish, last)
                if end_block:
                    end_block(ib)

            one_block(0, False, False)
            with eng.Fori(0, NB - 2) as before:
                one_block(before + 1, True, False)
            one_block(NB - 1, True, True)

        @block.sync
        def _(sp):
            sp.dma_start(wh[:, 0:NT, :].rearrange("p (i t) f -> p i (t f)", t=T),
                         x.rearrange("(i p t) f -> p i (t f)", p=P, t=T)).then_inc(x_in, 16)
            sp.dma_start(w_sb[:, :], W).then_inc(par_in, 16)
            sp.dma_start(a12[:, 0:1], a1).then_inc(par_in, 16)
            sp.dma_start(a12[:, 1:2], a2).then_inc(par_in, 16)
            sp.dma_start(b_sb[:, :], b).then_inc(par_in, 16)
            sp.dma_start(wcat[:, K * D:K * D + K], W1).then_inc(par_in, 16)
            sp.dma_start(wcat[:, 0:K * D].rearrange("c (k f) -> c k f", f=D),
                         W2.rearrange("k c f -> c k f")).then_inc(w2_in, 16)

            def turn(i, ib, jg, finish, last):
                for p in range(2):
                    for h in range(2):
                        q = 2 * p + h
                        sp.wait_ge(adj_cast[q], i)
                        sp.dma_start(adj_sb[:, q, :].rearrange("p (t n) -> p t n", n=BLK),
                                     adj_v[bass.ds(ib, 1), :, h * HT:(h + 1) * HT,
                                           bass.ds((2 * jg + p) * BLK, BLK)].rearrange("i p t n -> (i p) t n"))\
                          .then_inc(adj_in[q], 16)

            attention_loop(sp, turn)

            for q in range(4):
                sp.wait_ge(adj_cast[q], NB * IT)
            for p in range(2):
                sp.wait_ge(mt_stored[p], 16 * NB * IT)
                sp.wait_ge(whs_ready[p], NB * IT)
                sp.wait_ge(msg_out[p], 16 * (NB - 1) * IT)
            sp.wait_ge(turned, C * NB * NB)

            def load_messages(s):
                sp.dma_start(msgs[:, s * T:(s + 1) * T, :, :].rearrange("p n c f -> p (n c f)"),
                             msg_d[:, s * T:(s + 1) * T, :].rearrange("p n f -> p (n f)")).then_inc(msgs_in[s], 16)

            def load_masks(ii, s):
                q = s % 4
                if q < 3:
                    sp.wait_ge(masks_used[q], ii * (NB // 4) + s // 4)
                elif s == q:
                    sp.wait_ge(y_done, ii)
                else:
                    sp.wait_ge(masks_used[q], ii * (NB // 4 - 1) + s // 4)
                sp.dma_start(masks_w[:, q, :, :],
                             maskT_d[s, bass.ds(2 * ii, 2), :, :].rearrange("i p w -> p i w"))\
                  .then_inc(masks_in[q], 16)

            def load_kept(ii):
                sp.wait_ge(out_ready, ii * 4)
                sp.dma_start(keeps[:, :, :], keep_d[:, bass.ds(2 * T * ii, 2 * T), :]).then_inc(keeps_in, 16)

            for s in range(NB):
                if s == NB - 1:
                    for p in range(2):
                        sp.wait_ge(msg_out[p], 16 * NB * IT)
                        sp.wait_ge(keep_out[p], 16 * NB * IT)
                load_messages(s)
                load_masks(0, s)
            sp.wait_ge(p_used[3], 4 * NB * IT)
            load_kept(0)
            with sp.Fori(0, NB // 2 - 1) as before:
                for s in range(NB):
                    load_masks(before + 1, s)
                load_kept(before + 1)

        @block.gpsimd
        def _(pool):
            pool.memset(ident[:, :], 0.0).then_inc(consts, 1)
            pool.memset(ident16[:, :], 0.0).then_inc(consts, 1)
            pool.wait_ge(consts, 2)
            for m in (ident, ident16):
                pool.affine_select(out=m[:, :], in_=m[:, :], compare_op=ALU.not_equal, fill=1.0, base=0,
                                   pattern=[[-1, P]], channel_multiplier=1).then_inc(consts, 1)
            pool.memset(zeros16[:, :], 0.0).then_inc(consts, 1)
            pool.memset(ones[:, :], 1.0).then_inc(consts, 1)
            pool.memset(eps[:, :], EPS).then_inc(consts, 1)
            pool.memset(acc[:, :, :], 0.0).then_inc(acc_clear, 1)

            def copy_wh(p, step, use):
                pool.wait_ge(p_used[3], use)
                pool.sem_inc(past_pool, 1)
                pool.tensor_copy(whs[:, p, :, :], wh[:, bass.ds(step * T, T), :]).then_inc(whs_ready[p], 1)

            def finish_tile(p, u, m):
                for g in range(2):
                    pool.wait_ge(hw_scaled[g], 2 * m + 2)
                for r, n in enumerate((8, 4, 2)):
                    if r:
                        pool.wait_ge(fold_step, 3 * m + r)
                    pool.tensor_tensor(prod[:, 0:n, :], prod[:, 0:n, :], prod[:, n:2 * n, :], ALU.add)\
                        .then_inc(fold_step, 1)
                pool.wait_ge(fold_step, 3 * m + 3)
                pool.tensor_tensor(msg32[:, 0, :], prod[:, 0, :], prod[:, 1, :], ALU.add).then_inc(prod_read, 1)
                for part in range(3):
                    if part == 0:
                        pool.wait_ge(prod_read, m + 1)
                        pool.wait_ge(msg_out[p], 16 * u)
                    else:
                        pool.wait_ge(cut_step, 5 * m + 2 * part)
                    pool.sem_inc(past_pool, 1)
                    src, rest = msg32[:, part % 2, :], msg32[:, 1 - part % 2, :]
                    cut = msg[:, p, part * D:(part + 1) * D]
                    pool.tensor_copy(cut, src).then_inc(cut_step, 1)
                    pool.wait_ge(cut_step, 5 * m + 2 * part + 1)
                    if part < 2:
                        pool.tensor_tensor(rest, src, cut, ALU.subtract).then_inc(cut_step, 1)
                pool.dma_start(msg_d[:, bass.ds(m, 1), :], msg[:, p:p + 1, :]).then_inc(msg_out[p], 16)
                pool.wait_ge(node_copied, 2 * m + 2)
                pool.wait_ge(xn_done, m + 1)
                pool.dma_start(keep_d[:, bass.ds(m, 1), :], keep[:, p:p + 1, :]).then_inc(keep_out[p], 16)

            pool.wait_ge(wh_scaled, NB)
            copy_wh(0, 0, 0)

            def load_z(ib):
                pool.dma_start(zbf[:, bass.ds((ib % 2) * BLK, BLK)],
                               zrow_d[bass.ds(ib * T, T), :].rearrange("t p -> (t p)").partition_broadcast(P))\
                    .then_inc(zb_in, 16)

            pool.wait_ge(z_stored, 16)
            load_z(0)

            def start_block(ib, last):
                if not last:
                    pool.wait_ge(zb_in, 16 * (ib + 1))
                    pool.wait_ge(dve_step[1], ib * IT)
                    load_z(ib + 1)

            def turn(i, ib, jg, finish, last):
                for p in range(2):
                    if p == 0:
                        copy_wh(1, 2 * jg + 1, 4 * i)
                    elif not last:
                        copy_wh(0, 0 if isinstance(jg, int) else 2 * jg + 2, 4 * i + 2)
                    if finish:
                        u = i - IT
                        finish_tile(p, u, 2 * u + p)

            def end_block(ib):
                pool.wait_ge(den_done, ib + 1)
                pool.sem_inc(past_pool, 1)
                pool.memset(acc[:, :, :], 0.0).then_inc(acc_clear, 1)

            attention_loop(pool, turn, start_block, end_block)
            with pool.Fori(0, IT) as j:
                for p in range(2):
                    u = j + (NB - 1) * IT
                    finish_tile(p, u, 2 * u + p)

        @block.scalar
        def _(act):
            act.wait_ge(setup_pe, 2)
            act.activation(tr_sb[:, :], u_ps[:, 0:D], ACT.Copy).then_inc(setup_act, 1)
            act.activation(ut[0:K, HB:HB + D], u_ps[0:K, D:2 * D], ACT.Copy).then_inc(setup_act, 1)
            act.wait_ge(setup_pe, 4)
            act.activation(wa[:, :], h_ps[:, 0:2], ACT.Copy).then_inc(setup_act, 1)
            act.activation(wcat[:, K * D + K:], h_ps[:, D:2 * D], ACT.Copy).then_inc(setup_act, 1)
            act.wait_ge(consts, 7)
            with act.Fori(0, NB) as i:
                act.wait_ge(mv8_done, i + 1)
                act.activation(std8, mv8[:, :, 1], ACT.Sqrt, bias=eps[:, :]).then_inc(std8_done, 1)
                for g in range(2):
                    act.wait_ge(xnT_done, 2 * i + g + 1)
                    act.wait_ge(wh_done, 2 * i)
                    act.activation(hT4[:, g, :], mt_ps[g][:, :], ACT.Relu,
                                   accum_out=hsum[:, bass.ds(2 * i + g, 1)]).then_inc(hT_done, 1)
                for g in range(2):
                    act.wait_ge(wh_done, 2 * i + g + 1)
                    act.activation(wh[:, bass.ds(T * i + 4 * g, 4), :].rearrange("p t f -> p (t f)"),
                                   ot_ps[g][:, :], ACT.Copy).then_inc(wh_copied, 1)

            def cast(q, count, turned_before):
                act.wait_ge(adj_in[q], 16 * count)
                act.wait_ge(turned, turned_before)
                h = q % 2
                act.activation(m8[:, q // 2, h * HT:(h + 1) * HT, :].rearrange("p t n -> p (t n)"),
                               adj_sb[:, q, :], ACT.Copy, scale=EDGE).then_inc(adj_cast[q], 1)

            def evict(chunk, k, p, use):
                act.wait_ge(turned, chunk + 1)
                if k == 0:
                    act.wait_ge(dve_step[p], use)
                    act.wait_ge(mt_stored[p], 16 * use)
                act.activation(mt[:, p, k, :], mt_ps[k % 2][:, :].bitcast(U16), ACT.Copy).then_inc(evicted, 1)

            for q in range(3):
                cast(q, 1, 0)
            act.wait_ge(setup_dve, 13)
            act.activation(bcol[:, :], fcol[:, :, 1], ACT.Exp, bias=shifts[:, 0:1]).then_inc(setup_act, 1)
            act.activation(qcol[:, :], fcol[:, :, 1], ACT.Exp, bias=shifts[:, 1:2], scale=SLOPE - 1.0)\
               .then_inc(setup_act, 1)
            act.activation(zcol[:, :], zcol[:, :], ACT.Exp, scale=1.0 - SLOPE).then_inc(setup_act, 1)
            act.wait_ge(setup_pe, 8)
            act.activation(whsum[:, :], u_ps[:, 0:D], ACT.Copy).then_inc(setup_act, 1)
            act.activation(zT[:, :], u_ps[0:NT, D:D + P], ACT.Copy).then_inc(setup_act, 1)
            act.wait_ge(setup_act, 9)
            act.dma_start(zrow_d, zT[:, :]).then_inc(z_stored, 16)
            evict(0, 0, 0, 0)
            evict(1, 1, 0, 0)

            def finish_tile(k, p, u, m, t, pb):
                if k == 0:
                    act.wait_ge(u_done, m)
                    act.wait_ge(ot_copied, 2 * pb + 2)
                    act.activation(ustat[:, :], ut[:, bass.ds(t * P, P)], ACT.Copy).then_inc(u_copied, 1)
                elif k == 1:
                    act.wait_ge(mv_done, m + 1)
                    act.activation(std[:, :], mv[:, 1:2], ACT.Sqrt, bias=eps[:, :]).then_inc(std_done, 1)
                elif k == 2:
                    act.wait_ge(hps_done, m + 1)
                    act.activation(hT[:, :], h_ps[:, 0:D], ACT.Relu).then_inc(h_done, 1)
                    act.wait_ge(node_done, m + 1)
                    act.activation(node[:, :], NODE, ACT.Copy).then_inc(node_copied, 1)
                    act.wait_ge(keep_out[p], 16 * u)
                    act.activation(keep[:, p, D:2 * D], BIAS, ACT.Copy).then_inc(node_copied, 1)
                    act.wait_ge(node_copied, 2 * m + 2)
                    act.wait_ge(prod_read, m)
                if k >= 2:
                    for g in ((0, 1) if k == 2 else (2, 3)):
                        act.wait_ge(hw_done, 4 * m + g + 1)
                        for j in range(4):
                            head = 4 * g + j
                            ins = act.activation(prod[:, head, :], hw_ps[g % 2][:, j * D:(j + 1) * D], ACT.Copy,
                                                 scale=node[:, head:head + 1])
                        ins.then_inc(hw_scaled[g % 2], 1)

            def load_xt(pb):
                act.wait_ge(mv_done, T * pb)
                act.dma_start(xt[:, :, :], x_v[bass.ds(pb, 1)].rearrange("i p t f -> (i p) t f")).then_inc(xt_in, 16)

            def start_block(ib, last):
                if not (isinstance(ib, int) and ib == 0):
                    load_xt(ib - 1)

            def turn(i, ib, jg, finish, last):
                for p in range(2):
                    n = 2 * i + p
                    for k in range(C):
                        if k < 2:
                            evict(C * n + k + 2, k + 2, p, 0)
                        elif not (last and p == 1):
                            evict(C * n + k + 2, k - 2, 1 - p, i + p)
                        if k == 2:
                            act.wait_ge(evicted, C * n + C)
                            act.dma_start(maskT_d[bass.ds(2 * jg + p, 1), bass.ds(ib, 1), :, :]
                                          .rearrange("s i p w -> (s i p) w"),
                                          mt[:, p, :, :].rearrange("p c n -> p (c n)")).then_inc(mt_stored[p], 16)
                        if finish:
                            u = i - IT
                            finish_tile(k, p, u, 2 * u + p, 2 * jg + p, ib - 1)
                        if k == 1 and not (last and p == 1):
                            cast(3 if p == 0 else 1, i + 1 + p, C * n)
                        if k == 3 and not last:
                            cast(2 * p, i + 2, C * n + C)

            def end_block(ib):
                act.wait_ge(p_used[3], 4 * IT * (ib + 1))
                for h in range(2):
                    act.activation(ut[:, h * HB:(h + 1) * HB], ot_ps[h][:, :], ACT.Copy).then_inc(ot_copied, 1)

            attention_loop(act, turn, start_block, end_block)
            load_xt(NB - 1)
            with act.Fori(0, IT) as j:
                for p in range(2):
                    u = j + (NB - 1) * IT
                    for k in range(C):
                        finish_tile(k, p, u, 2 * u + p, 2 * j + p, NB - 1)

            act.wait_ge(prod_read, NT)
            with act.Fori(0, NB // 2) as ii:
                act.wait_ge(y_done, ii + 1)
                act.wait_ge(y_turned, 4 * ii)
                for h in range(2):
                    act.activation(yT[:, h * HB:(h + 1) * HB], acc_ps[h][:, :], ACT.Copy, scale=1.0 / EDGE_FP8)\
                       .then_inc(y_act, 1)
                for h in range(2):
                    act.wait_ge(out_ready, 4 * ii + 2 * h + 2)
                    act.dma_start(out_v[bass.ds(2 * ii + h, 1)].rearrange("i p t f -> (i p) t f"),
                                  outs[:, h * T:(h + 1) * T, :]).then_inc(out_stored, 16)
            act.wait_ge(out_stored, 16 * NB)

        @block.tensor
        def _(pe):
            pe.wait_ge(consts, 7)
            pe.wait_ge(par_in, 80)
            pe.transpose(u_ps[:, 0:D], w_sb[:, :], ident[:, :]).then_inc(setup_pe, 1)
            pe.transpose(u_ps[0:K, D:2 * D], wcat[:, K * D:K * D + K], ident[:, :]).then_inc(setup_pe, 1)
            pe.wait_ge(setup_act, 2)
            pe.matmul(h_ps[:, 0:2], tr_sb[:, :], a12[:, :], start=True, stop=True).then_inc(setup_pe, 1)
            pe.matmul(h_ps[:, D:2 * D], ut[0:K, HB:HB + D], b_sb[:, :], start=True, stop=True).then_inc(setup_pe, 1)
            pe.wait_ge(setup_act, 4)
            with pe.Fori(0, NB) as i:
                pe.wait_ge(xn8_done, i + 1)
                pe.wait_ge(hT_done, 2 * i)
                for g in range(2):
                    for j in range(4):
                        ins = pe.transpose(mt_ps[g][:, j * D:(j + 1) * D], xn8[:, 4 * g + j, :], ident[:, :])
                    ins.then_inc(xnT_done, 1)
                for g in range(2):
                    pe.wait_ge(hT_done, 2 * i + g + 1)
                    pe.wait_ge(wh_copied, 2 * i)
                    for j in range(4):
                        rows = hT4[:, g, j * P:(j + 1) * P]
                        pe.matmul(ot_ps[g][:, j * D:(j + 1) * D], rows, w_sb[:, :], start=True, stop=True)
                        ins = pe.matmul(hw_ps[0][:, bass.ds(2 * T * i + 8 * g + 2 * j, 2)], rows, wa[:, :],
                                        start=True, stop=True)
                    ins.then_inc(wh_done, 1)
            pe.wait_ge(setup_dve, 4)
            pe.transpose(h_ps[0:2, 0:P], ext[:, :], ident[:, :]).then_inc(setup_pe, 1)
            pe.wait_ge(setup_dve, 6)
            pe.matmul(h_ps[:, HB // 2:HB // 2 + 2], ones[0:2, :], extd[:, :], start=True, stop=True)\
              .then_inc(setup_pe, 1)
            pe.wait_ge(setup_dve, 13)
            pe.matmul(u_ps[:, 0:D], hrep[:, :], w_sb[:, :], start=True, stop=True).then_inc(setup_pe, 1)
            pe.wait_ge(setup_act, 7)
            pe.transpose(u_ps[0:NT, D:D + P], zcol[:, :], ident[:, :]).then_inc(setup_pe, 1)

            def turn_mask(chunk, k, p, casts):
                if k == 0:
                    for h in range(2):
                        pe.wait_ge(adj_cast[2 * p + h], casts)
                if not (isinstance(chunk, int) and chunk < 2):
                    pe.wait_ge(evicted, chunk - 1)
                words = mt_ps[k % 2][:, :].bitcast(BF16)
                for t in range(T):
                    ins = pe.transpose(words[:, t * P:(t + 1) * P],
                                       m8[:, p, t, :].bitcast(BF16)[:, k:BLK // 2:C], ident16[:, :])
                ins.then_inc(turned, 1)

            turn_mask(0, 0, 0, 1)
            turn_mask(1, 1, 0, 1)

            def finish_tile(k, m, pb):
                if k == 0:
                    pe.wait_ge(u_copied, m + 1)
                    pe.wait_ge(u_read, m)
                    pe.wait_ge(den_read, pb + 1)
                    pe.transpose(u_ps[:, 0:D], ustat[:, :], ident[:, :]).then_inc(u_done, 1)
                elif k == 2:
                    pe.wait_ge(h_done, m + 1)
                    pe.matmul(h_ps[:, D:D + K + D], hT[:, :], wcat[:, K * D:], start=True, stop=True)\
                      .then_inc(node_done, 1)
                if k >= 2:
                    for g in ((0, 1) if k == 2 else (2, 3)):
                        pe.wait_ge(hw_scaled[g % 2], 2 * m + g // 2)
                        pe.matmul(hw_ps[g % 2][:, :], hT[:, :], wcat[:, g * HB:(g + 1) * HB], start=True, stop=True)\
                          .then_inc(hw_done, 1)

            def finish_turn_h(m):
                pe.wait_ge(xn_done, m + 1)
                pe.wait_ge(node_copied, 2 * m)
                pe.transpose(h_ps[:, 0:D], xn[:, :], ident[:, :]).then_inc(hps_done, 1)

            pe.wait_ge(w2_in, 16)

            def start_block(ib, last):
                pe.wait_ge(ot_copied, 2 * ib)
                for h in range(2):
                    pe.matmul(ot_ps[h][:, :], zeros16[:, 0:P], zeros16[:, :], start=True, stop=False)

            def turn(i, ib, jg, finish, last):
                for p in range(2):
                    n = 2 * i + p
                    m = 2 * (i - IT) + p
                    for k in range(C):
                        if k < 2:
                            turn_mask(C * n + k + 2, k + 2, p, 0)
                        elif not (last and p == 1):
                            turn_mask(C * n + k + 2, k - 2, 1 - p, i + 1 + p)
                        if finish and k == 2:
                            finish_turn_h(m)
                        if k == 0:
                            pe.wait_ge(whs_ready[p], i + 1)
                        for b_ in range(2):
                            r = 2 * (k % 2) + b_
                            pe.wait_ge(p_ready, 2 * (C * n + k) + b_ + 1)
                            end = isinstance(jg, int) and p == 1 and k == C - 1 and b_ == 1
                            for h in range(2):
                                ins = pe.matmul(ot_ps[h][:, :], whs[:, p, 2 * k + b_, :],
                                                p_sb[:, r, h * HB:(h + 1) * HB], start=False, stop=end)
                            ins.then_inc(p_used[r], 1)
                        if finish:
                            finish_tile(k, m, ib - 1)

            def end_block(ib):
                pe.wait_ge(dve_step[1], IT * (ib + 1))
                pe.wait_ge(u_read, T * ib)
                for t in range(T):
                    for h in range(2):
                        ins = pe.matmul(DEN[:, t:t + 1], acc[:, h, t * P:(t + 1) * P], ones[:, 0:1],
                                        start=h == 0, stop=h == 1)
                ins.then_inc(den_done, 1)

            attention_loop(pe, turn, start_block, end_block)

            stages = [(m, k) for m in range((NB - 1) * T, NT) for k in range(C)]
            slots = (NB - 1) * T - 6

            def gather(ii, first):
                done = 0
                for s in range(NB):
                    q = s % 4
                    pe.wait_ge(msgs_in[s], 16)
                    pe.wait_ge(masks_in[q], 16 * (ii * (NB // 4) + s // 4 + 1))
                    pe.sem_inc(past_pe, 1)
                    for t in range(T):
                        for c in range(3):
                            for ib in range(2):
                                for h in range(2):
                                    ins = pe.matmul(acc_ps[2 * ib + h][:, :], msgs[:, s * T + t, c, :],
                                                    masks[:, q, ib, t // 2, h * HB:(h + 1) * HB, t % 2],
                                                    start=s == 0 and t == 0 and c == 0,
                                                    stop=s == NB - 1 and t == T - 1 and c == 2)
                        if t == T - 1:
                            if s < NB - 1:
                                ins.then_inc(masks_used[q], 1)
                            else:
                                ins.then_inc(y_done, 1)
                        while first and done < len(stages) and (s * T + t + 1) * len(stages) >= (done + 1) * slots:
                            m, k = stages[done]
                            if k == 2:
                                finish_turn_h(m)
                            finish_tile(k, m, NB - 1)
                            done += 1
                pe.wait_ge(out_ready, 4 * ii)
                for g in range(4):
                    pe.wait_ge(y_act if g < 2 else y_dve, 2 * ii + g % 2 + 1)
                    for j in range(4):
                        ins = pe.transpose(y_ps[g][:, j * P:(j + 1) * P],
                                           yT[:, (4 * g + j) * P:(4 * g + j + 1) * P], ident[:, :])
                    ins.then_inc(y_turned, 1)

            pe.wait_ge(ot_copied, 2 * NB)
            pe.wait_ge(evicted, C * NB * NB)
            gather(0, True)
            with pe.Fori(0, NB // 2 - 1) as before:
                gather(before + 1, False)

        @block.vector
        def _(dve):
            dve.wait_ge(x_in, 16)
            with dve.Fori(0, NB) as i:
                for t in range(T):
                    ins = dve.bn_stats(stat8[:, t, :], wh[:, bass.ds(T * i + t, 1), :].rearrange("p t f -> p (t f)"))
                ins.then_inc(stats8, 1)
                dve.wait_ge(stats8, i + 1)
                dve.sem_inc(past_dve, 1)
                for t in range(T):
                    ins = dve.bn_aggr(mv8[:, t, :], stat8[:, t, :])
                ins.then_inc(mv8_done, 1)
                dve.wait_ge(std8_done, i + 1)
                dve.reciprocal(rstd8, std8).then_inc(rstd8_done, 1)
                dve.wait_ge(rstd8_done, i + 1)
                dve.wait_ge(xnT_done, 2 * i)
                for t in range(T):
                    ins = dve.tensor_scalar(xn8[:, t, :], wh[:, bass.ds(T * i + t, 1), :]
                                            .rearrange("p t f -> p (t f)"),
                                            mv8[:, t, 0:1], rstd8[:, t:t + 1], ALU.subtract, ALU.mult)
                ins.then_inc(xn8_done, 1)
            dve.wait_ge(wh_done, 2 * NB)
            dve.tensor_copy(fcol[:, :, :].rearrange("p n c -> p (n c)"), hw_ps[0][:, 0:2 * NT]).then_inc(setup_dve, 1)
            dve.wait_ge(setup_dve, 1)
            dve.tensor_reduce(ext[:, 0:1], fcol[:, :, 1], AX.X, ALU.max).then_inc(setup_dve, 1)
            dve.tensor_reduce(ext[:, 1:2], fcol[:, :, 1], AX.X, ALU.min).then_inc(setup_dve, 1)
            dve.wait_ge(setup_dve, 3)
            dve.tensor_scalar(ext[:, 1:2], ext[:, 1:2], -1.0, None, ALU.mult).then_inc(setup_dve, 1)
            dve.wait_ge(setup_pe, 5)
            dve.tensor_reduce(ext2[:, :], h_ps[0:2, 0:P], AX.X, ALU.max).then_inc(setup_dve, 1)
            dve.wait_ge(setup_dve, 5)
            dve.tensor_scalar(extd[:, :], ident[0:2, 0:2], ext2[:, 0:1], None, ALU.mult).then_inc(setup_dve, 1)
            dve.wait_ge(setup_pe, 6)
            dve.tensor_copy(gmm[:, :], h_ps[:, HB // 2:HB // 2 + 2]).then_inc(setup_dve, 1)
            dve.wait_ge(setup_dve, 7)
            dve.tensor_scalar(shifts[:, 0:1], gmm[:, 0:1], -1.0, None, ALU.mult).then_inc(setup_dve, 1)
            dve.tensor_scalar(shifts[:, 1:2], gmm[:, 0:1], 1.0 - SLOPE, None, ALU.mult).then_inc(setup_dve, 1)
            dve.tensor_tensor(shifts[:, 2:3], gmm[:, 0:1], gmm[:, 1:2], ALU.add).then_inc(setup_dve, 1)
            dve.tensor_reduce(hsum1[:, :], hsum[:, :], AX.X, ALU.add).then_inc(setup_dve, 1)
            dve.wait_ge(setup_dve, 11)
            dve.tensor_scalar(zcol[:, :], fcol[:, :, 0], gmm[:, 0:1], shifts[:, 2:3], ALU.add, ALU.min)\
               .then_inc(setup_dve, 1)
            dve.tensor_scalar(hrep[:, :], ones[:, :], hsum1[:, :], None, ALU.mult).then_inc(setup_dve, 1)
            dve.wait_ge(wh_copied, 2 * NB)
            dve.wait_ge(setup_act, 5)
            with dve.Fori(0, NB) as i:
                rows = wh[:, bass.ds(T * i, T), :]
                dve.tensor_tensor(rows, rows, bcol[:, bass.ds(T * i, T)].unsqueeze(2).to_broadcast([P, T, D]),
                                  ALU.mult).then_inc(wh_scaled, 1)
            dve.wait_ge(setup_act, 9)

            def finish_tile(k, p, u, m, t, pb):
                x1 = keep[:, p, 0:D]
                if k == 1:
                    dve.wait_ge(u_done, m + 1)
                    dve.scalar_tensor_tensor(att[:, :], whsum[:, :], empty[:, bass.ds(t, 1)], u_ps[:, 0:D],
                                             ALU.mult, ALU.add).then_inc(u_read, 1)
                    dve.wait_ge(u_read, m + 1)
                    dve.tensor_scalar(att[:, :], att[:, :], rden[:, bass.ds(t, 1)], 0.0, ALU.mult, ALU.max)\
                       .then_inc(x1_step, 1)
                    dve.wait_ge(x1_step, 3 * m + 1)
                    dve.wait_ge(xt_in, 16 * (pb + 1))
                    dve.wait_ge(keep_out[p], 16 * u)
                    dve.tensor_tensor(x1, att[:, :], xt[:, bass.ds(t, 1), :].rearrange("p t f -> p (t f)"), ALU.add)\
                       .then_inc(x1_step, 1)
                    dve.wait_ge(x1_step, 3 * m + 2)
                    dve.bn_stats(stat[:, :], x1).then_inc(x1_step, 1)
                    dve.wait_ge(x1_step, 3 * m + 3)
                    dve.sem_inc(past_dve, 1)
                    dve.bn_aggr(mv[:, :], stat[:, :]).then_inc(mv_done, 1)
                elif k == 2:
                    dve.wait_ge(std_done, m + 1)
                    dve.reciprocal(rstd[:, :], std[:, :]).then_inc(rstd_done, 1)
                    dve.wait_ge(rstd_done, m + 1)
                    dve.wait_ge(hps_done, m)
                    dve.tensor_scalar(xn[:, :], x1, mv[:, 0:1], rstd[:, :], ALU.subtract, ALU.mult)\
                       .then_inc(xn_done, 1)

            def start_block(ib, last):
                dve.wait_ge(zb_in, 16 * (ib + 1))
                dve.sem_inc(past_dve, 1)

            def turn(i, ib, jg, finish, last):
                for p in range(2):
                    n = 2 * i + p
                    u = i - IT
                    for k in range(C):
                        c = C * n + k
                        tile = (2 * jg + p) * T + 2 * k
                        dve.wait_ge(evicted, c + 1)
                        for b_ in range(2):
                            r = 2 * (k % 2) + b_
                            dve.wait_ge(p_used[r], 4 * i + 2 * p + k // 2)
                            dve.scalar_tensor_tensor(p_sb[:, r, :], zbf[:, bass.ds((ib % 2) * BLK, BLK)],
                                                     qcol[:, bass.ds(tile + b_, 1)], mtb[:, p, k, :, b_],
                                                     ALU.max, ALU.mult).then_inc(p_ready, 1)
                        if finish and k == 1:
                            finish_tile(1, p, u, 2 * u + p, 2 * jg + p, ib - 1)
                        if k == 0 and p == 0:
                            dve.wait_ge(acc_clear, ib + 1)
                        for b_ in range(2):
                            r = 2 * (k % 2) + b_
                            dve.wait_ge(p_ready, 2 * c + b_ + 1)
                            ins = dve.scalar_tensor_tensor(acc[:, b_, :], p_sb[:, r, :],
                                                           bcol[:, bass.ds(tile + b_, 1)], acc[:, b_, :],
                                                           ALU.mult, ALU.add)
                        if finish and k == 1:
                            finish_tile(2, p, u, 2 * u + p, 2 * jg + p, ib - 1)
                    ins.then_inc(dve_step[p], 1)

            def end_block(ib):
                dve.wait_ge(den_done, ib + 1)
                dve.tensor_scalar(empty[:, :], DEN, 0.0, None, ALU.is_equal).then_inc(den_step, 1)
                dve.wait_ge(den_step, 2 * ib + 1)
                dve.scalar_tensor_tensor(den[:, :], empty[:, :], float(N), DEN, ALU.mult, ALU.add)\
                   .then_inc(den_step, 1)
                dve.wait_ge(den_step, 2 * ib + 2)
                dve.reciprocal(rden[:, :], den[:, :]).then_inc(den_read, 1)

            attention_loop(dve, turn, start_block, end_block)
            with dve.Fori(0, IT) as j:
                for p in range(2):
                    u = j + (NB - 1) * IT
                    for k in range(1, 3):
                        finish_tile(k, p, u, 2 * u + p, 2 * j + p, NB - 1)

            dve.wait_ge(prod_read, NT)
            with dve.Fori(0, NB // 2) as ii:
                dve.wait_ge(y_done, ii + 1)
                dve.wait_ge(y_turned, 4 * ii)
                for h in range(2, 4):
                    dve.tensor_scalar(yT[:, h * HB:(h + 1) * HB], acc_ps[h][:, :], 1.0 / EDGE_FP8, None, ALU.mult)\
                       .then_inc(y_dve, 1)
                dve.wait_ge(keeps_in, 16 * (ii + 1))
                dve.wait_ge(out_stored, 32 * ii)
                for g in range(4):
                    rows = outs[:, 4 * g:4 * g + 4, :]
                    dve.wait_ge(y_turned, 4 * ii + g + 1)
                    dve.tensor_tensor(rows, y_ps[g][:, :].rearrange("p (n f) -> p n f", f=D),
                                      keeps[:, 4 * g:4 * g + 4, D:2 * D], ALU.add).then_inc(y_step, 1)
                    dve.wait_ge(y_step, 4 * ii + g + 1)
                    dve.scalar_tensor_tensor(rows, rows, 0.0, keeps[:, 4 * g:4 * g + 4, 0:D], ALU.max, ALU.add)\
                       .then_inc(out_ready, 1)


_INS = ["x", "adj", "L0_gnn_W", "L0_gnn_a1", "L0_gnn_a2", "L1_gnn_W1", "L1_gnn_W2", "L1_gnn_b"]


def kernel(**inputs):
    import numpy as _np
    import concourse.bacc as _bacc
    from concourse.bass_utils import run_bass_kernel_spmd as _run

    nc = _bacc.Bacc("TRN2", target_bir_lowering=False, num_devices=1)
    arrays, args = {}, []
    for name in _INS:
        a = _np.ascontiguousarray(inputs[name])
        arrays[f"in_{name}_dram"] = a
        args.append(nc.dram_tensor(f"in_{name}_dram", a.shape, mybir.dt.from_np(a.dtype), kind="ExternalInput").ap())
    shape = inputs["x"].shape
    args.append(nc.dram_tensor("out_0_dram", shape, FP32, kind="ExternalOutput").ap())
    build(nc, *args)
    r = _run(nc, [arrays], core_ids=[0])
    return r.results[0]["out_0_dram"]
```
